# Optimizing a Trainium2 kernel written in Bass

```python
import numpy as np
import jax
import jax.numpy as jnp

def _softmax(x, axis=-1):
    return jax.nn.softmax(x, axis=axis)

def _gelu(x):
    return jax.nn.gelu(x, approximate=True)

def _silu(x):
    return jax.nn.silu(x)

def _sigmoid(x):
    return jax.nn.sigmoid(x)

def _layernorm(x, axis=-1, eps=1e-05):
    m = jnp.mean(x, axis=axis, keepdims=True)
    v = jnp.var(x, axis=axis, keepdims=True)
    return (x - m) / jnp.sqrt(v + eps)

def _scatter_add(tgt, idx, src, axis=0):
    return tgt.at[idx].add(src)

def _segment_sum(src, seg, n):
    return jax.ops.segment_sum(src, seg, n)
kernel_name = 'mk_gnn_resnorm_d4_gnn_r32_ed7af1'

def setup_inputs(seed: int=0):
    np.random.seed(seed)
    _w = jnp.asarray

    def _rec_inputs():
        import jax
        import jax.numpy as jnp
        _gk = jax.random.key(seed)
        x = -0.0002117 + 1 * jax.random.normal(jax.random.fold_in(_gk, 1), (3125, 256), jnp.float32)
        src = jax.random.randint(jax.random.fold_in(_gk, 2), (50000,), 0, 3125, jnp.int32)
        dst = jnp.minimum((3125 * jax.random.uniform(jax.random.fold_in(_gk, 3), (50000,)) ** 2.0).astype(jnp.int32), 99999)
        _o = jnp.argsort(dst, stable=True)
        src = src[_o]
        dst = dst[_o]
        edge_type_8 = jax.random.randint(jax.random.fold_in(_gk, 13), (50000,), 0, 8, jnp.int32)
        edge_weight = jax.random.uniform(jax.random.fold_in(_gk, 14), (50000,), jnp.float32, 0.0, 1)
        return (x, src, dst, edge_type_8, edge_weight)
    x, src, dst, edge_type_8, edge_weight = _rec_inputs()

    def _L0_gnn_setup():
        import jax, jax.numpy as jnp
        import numpy as np
        N_NODES = 3125
        N_EDGES = 100000
        D_IN = 256
        D_OUT = 256
        key = jax.random.key(seed)
        k1, k2, k3, k4, k5, k6 = jax.random.split(key, 6)
        bound = 1.0 / np.sqrt(D_OUT)
        x = jax.random.normal(k1, (N_NODES, D_IN), dtype=jnp.float32)
        weight = jax.random.uniform(k2, (D_IN, D_OUT), dtype=jnp.float32, minval=-bound, maxval=bound)
        bias = jax.random.uniform(k3, (D_OUT,), dtype=jnp.float32, minval=-bound, maxval=bound)
        edge_src = jax.random.randint(k4, (N_EDGES,), 0, N_NODES, dtype=jnp.int32)
        edge_dst = jax.random.randint(k5, (N_EDGES,), 0, N_NODES, dtype=jnp.int32)
        edge_weight = jax.random.uniform(k6, (N_EDGES,), dtype=jnp.float32)
        return {'x': x, 'weight': weight, 'bias': bias, 'edge_src': edge_src, 'edge_dst': edge_dst, 'edge_weight': edge_weight}
    _L0_gnn_all = _L0_gnn_setup()
    _L0_gnn_in = {k: v for k, v in _L0_gnn_all.items() if k in ('weight', 'bias')}
    del _L0_gnn_all

    def _L1_gnn_setup():
        import jax, jax.numpy as jnp
        import numpy as np
        N_NODES = 50000
        N_EDGES = 25000
        IN_DIM = 256
        HID = 512
        N_LAYERS = 3
        OUT_DIM = 256
        TOTAL_HID = HID * (N_LAYERS + 1)
        key = jax.random.key(seed)
        ks = jax.random.split(key, 10)
        s = 0.02
        return {'x': jax.random.normal(ks[0], (N_NODES, IN_DIM), dtype=jnp.float32), 'edge_index': jax.random.randint(ks[1], (2, N_EDGES), 0, N_NODES, dtype=jnp.int64), 'in_W': jax.random.normal(ks[2], (IN_DIM, HID), dtype=jnp.float32) * s, 'in_b': jnp.zeros((HID,), dtype=jnp.float32), 'conv_W1': jax.random.normal(ks[3], (N_LAYERS, HID, HID), dtype=jnp.float32) * s, 'conv_b1': jnp.zeros((N_LAYERS, HID), dtype=jnp.float32), 'conv_W2': jax.random.normal(ks[4], (N_LAYERS, HID, HID), dtype=jnp.float32) * s, 'conv_b2': jnp.zeros((N_LAYERS, HID), dtype=jnp.float32), 'out_W': jax.random.normal(ks[5], (TOTAL_HID, OUT_DIM), dtype=jnp.float32) * s, 'out_b': jnp.zeros((OUT_DIM,), dtype=jnp.float32)}
    _L1_gnn_all = _L1_gnn_setup()
    _L1_gnn_in = {k: v for k, v in _L1_gnn_all.items() if k in ('in_W', 'in_b', 'conv_W1', 'conv_b1', 'conv_W2', 'conv_b2', 'out_W', 'out_b')}
    del _L1_gnn_all

    def _L2_gnn_setup():
        import jax, jax.numpy as jnp
        import numpy as np
        N_NODES = 625
        N_EDGES = 10000
        NUM_RELS = 8
        DIM = 256
        BN_EPS = 1e-05
        key = jax.random.key(seed)
        k1, k2, k3, k4, k5 = jax.random.split(key, 5)
        h = jax.random.normal(k1, (N_NODES, DIM), dtype=jnp.float32)
        weight = jax.random.normal(k2, (NUM_RELS, DIM, DIM), dtype=jnp.float32) * 0.05
        gamma = jnp.ones((DIM,), dtype=jnp.float32)
        beta = jnp.zeros((DIM,), dtype=jnp.float32)
        src = jax.random.randint(k3, (N_EDGES,), 0, N_NODES, dtype=jnp.int32)
        dst = jax.random.randint(k4, (N_EDGES,), 0, N_NODES, dtype=jnp.int32)
        rel = jax.random.randint(k5, (N_EDGES,), 0, NUM_RELS, dtype=jnp.int32)
        return {'h': h, 'weight': weight, 'gamma': gamma, 'beta': beta, 'src': src, 'dst': dst, 'rel': rel}
    _L2_gnn_all = _L2_gnn_setup()
    _L2_gnn_in = {k: v for k, v in _L2_gnn_all.items() if k in ('weight', 'gamma', 'beta')}
    del _L2_gnn_all

    def _L3_gnn_setup():
        import jax, jax.numpy as jnp
        import numpy as np
        N_NODES = 512
        D_FEAT = 256
        N_EDGES = 8192
        HIDDEN = 512
        D_OUT = 256
        key = jax.random.key(seed)
        ks = jax.random.split(key, 5)
        x = jax.random.normal(ks[0], (N_NODES, D_FEAT), dtype=jnp.float32)
        W1 = jax.random.normal(ks[1], (2 * D_FEAT, HIDDEN), dtype=jnp.float32) * (1.0 / np.sqrt(2 * D_FEAT))
        b1 = jnp.zeros((HIDDEN,), dtype=jnp.float32)
        W2 = jax.random.normal(ks[2], (HIDDEN, D_OUT), dtype=jnp.float32) * (1.0 / np.sqrt(HIDDEN))
        b2 = jnp.zeros((D_OUT,), dtype=jnp.float32)
        nn_index = jax.random.randint(ks[3], (2, N_EDGES), 0, N_NODES, dtype=jnp.int64)
        return {'x': x, 'W1': W1, 'b1': b1, 'W2': W2, 'b2': b2, 'nn_index': nn_index, 'k': 16}
    _L3_gnn_all = _L3_gnn_setup()
    _L3_gnn_in = {k: v for k, v in _L3_gnn_all.items() if k in ('W1', 'b1', 'W2', 'b2')}
    del _L3_gnn_all
    return {'x': x, 'src': src, 'dst': dst, 'edge_type_8': edge_type_8, 'edge_weight': edge_weight, 'L0_gnn_weight': _L0_gnn_in['weight'], 'L0_gnn_bias': _L0_gnn_in['bias'], 'L1_gnn_in_W': _L1_gnn_in['in_W'], 'L1_gnn_in_b': _L1_gnn_in['in_b'], 'L1_gnn_conv_W1': _L1_gnn_in['conv_W1'], 'L1_gnn_conv_b1': _L1_gnn_in['conv_b1'], 'L1_gnn_conv_W2': _L1_gnn_in['conv_W2'], 'L1_gnn_conv_b2': _L1_gnn_in['conv_b2'], 'L1_gnn_out_W': _L1_gnn_in['out_W'], 'L1_gnn_out_b': _L1_gnn_in['out_b'], 'L2_gnn_weight': _L2_gnn_in['weight'], 'L2_gnn_gamma': _L2_gnn_in['gamma'], 'L2_gnn_beta': _L2_gnn_in['beta'], 'L3_gnn_W1': _L3_gnn_in['W1'], 'L3_gnn_b1': _L3_gnn_in['b1'], 'L3_gnn_W2': _L3_gnn_in['W2'], 'L3_gnn_b2': _L3_gnn_in['b2']}

def reference(x, src, dst, edge_type_8, edge_weight, L0_gnn_weight, L0_gnn_bias, L1_gnn_in_W, L1_gnn_in_b, L1_gnn_conv_W1, L1_gnn_conv_b1, L1_gnn_conv_W2, L1_gnn_conv_b2, L1_gnn_out_W, L1_gnn_out_b, L2_gnn_weight, L2_gnn_gamma, L2_gnn_beta, L3_gnn_W1, L3_gnn_b1, L3_gnn_W2, L3_gnn_b2):
    import jax
    import jax.numpy as jnp

    def _L0_gnn_ref(x, weight, bias, edge_src, edge_dst, edge_weight):
        import jax, jax.numpy as jnp
        import numpy as np
        N_NODES = 3125
        N_EDGES = 100000
        D_IN = 256
        D_OUT = 256
        xw = jnp.matmul(x, weight)
        msgs = xw[edge_src] * edge_weight[:, None]
        z = jax.ops.segment_sum(msgs, edge_dst, num_segments=N_NODES)
        return z + bias

    def _L1_gnn_ref(x, edge_index, in_W, in_b, conv_W1, conv_b1, conv_W2, conv_b2, out_W, out_b):
        import jax, jax.numpy as jnp
        import numpy as np
        N_NODES = 50000
        N_EDGES = 25000
        IN_DIM = 256
        HID = 512
        N_LAYERS = 3
        OUT_DIM = 256
        TOTAL_HID = HID * (N_LAYERS + 1)
        src, dst = (edge_index[0], edge_index[1])
        n = x.shape[0]
        h = x @ in_W + in_b
        hidden_states = [h]
        for i in range(N_LAYERS):
            agg = jax.ops.segment_sum(h[src], dst, num_segments=n)
            z = h + agg
            z = jax.nn.relu(z @ conv_W1[i] + conv_b1[i])
            h = z @ conv_W2[i] + conv_b2[i]
            hidden_states.append(h)
        cat = jnp.concatenate(hidden_states, axis=1)
        return cat @ out_W + out_b

    def _L2_gnn_ref(h, weight, gamma, beta, src, dst, rel):
        import jax, jax.numpy as jnp
        import numpy as np
        N_NODES = 625
        N_EDGES = 10000
        NUM_RELS = 8
        DIM = 256
        BN_EPS = 1e-05
        all_h = jnp.einsum('ni,rio->nro', h, weight)
        msg = all_h[src, rel]
        agg = jax.ops.segment_sum(msg, dst, num_segments=h.shape[0])
        mean = jnp.mean(agg, axis=0)
        var = jnp.mean(jnp.square(agg - mean), axis=0)
        out = (agg - mean) * jax.lax.rsqrt(var + BN_EPS) * gamma + beta
        return out

    def _L3_gnn_ref(x, W1, b1, W2, b2, nn_index, k):
        import jax, jax.numpy as jnp
        import numpy as np
        N_NODES = 512
        D_FEAT = 256
        N_EDGES = 8192
        HIDDEN = 512
        D_OUT = 256
        num_nodes = x.shape[0]
        src = nn_index[0]
        tgt = nn_index[1]
        x_i = x[tgt]
        x_j = x[src]
        feat = jnp.concatenate([x_i, x_j - x_i], axis=-1)
        h = jax.nn.relu(feat @ W1 + b1)
        msg = h @ W2 + b2
        out = jax.ops.segment_sum(msg, tgt, num_segments=num_nodes)
        deg = jax.ops.segment_sum(jnp.ones((msg.shape[0], 1), dtype=msg.dtype), tgt, num_segments=num_nodes)
        return out / (deg + 1e-08)
    edge_index = jnp.stack([src, dst])
    x = _layernorm(x + _L0_gnn_ref(x, L0_gnn_weight, L0_gnn_bias, src, dst, edge_weight), axis=-1)
    x = _layernorm(x + _L1_gnn_ref(x, edge_index, L1_gnn_in_W, L1_gnn_in_b, L1_gnn_conv_W1, L1_gnn_conv_b1, L1_gnn_conv_W2, L1_gnn_conv_b2, L1_gnn_out_W, L1_gnn_out_b), axis=-1)
    x = _layernorm(x + _L2_gnn_ref(x, L2_gnn_weight, L2_gnn_gamma, L2_gnn_beta, src, dst, edge_type_8), axis=-1)
    x = _layernorm(x + _L3_gnn_ref(x, L3_gnn_W1, L3_gnn_b1, L3_gnn_W2, L3_gnn_b2, edge_index, 16), axis=-1)
    return x

_drawn_inputs = setup_inputs


def setup_inputs(seed=0):
    import zlib

    import numpy as np

    out = dict(_drawn_inputs(seed))
    spreads = {'L1_gnn_in_b': (0.0, 0.1),
     'L1_gnn_conv_b1': (0.0, 0.1),
     'L1_gnn_conv_b2': (0.0, 0.1),
     'L1_gnn_out_b': (0.0, 0.1),
     'L2_gnn_gamma': (1.0, 0.2),
     'L2_gnn_beta': (0.0, 0.1),
     'L3_gnn_b1': (0.0, 0.1),
     'L3_gnn_b2': (0.0, 0.1)}
    factors = {}
    for name, (base, spread) in spreads.items():
        noise = np.random.default_rng([zlib.crc32(name.encode()), seed]).standard_normal(out[name].shape)
        drawn = base * np.exp(spread * noise) if base else spread * noise
        out[name] = jnp.asarray(drawn.astype(out[name].dtype))
    for name, factor in factors.items():
        out[name] = (out[name] * factor).astype(out[name].dtype)
    return out
```

```python
from contextlib import ExitStack

import concourse.bass as bass
from concourse import mybir

P = 128
N_NODES, D, HID, RELS, EDGES = 3125, 256, 512, 8, 50000
NB = -(-N_NODES // P)
TAIL = N_NODES - (NB - 1) * P
T = 4
CE = T * P
NC = -(-EDGES // CE)
LAST = EDGES - (NC - 1) * CE
EPS = 1e-5

F32 = mybir.dt.float32
I32 = mybir.dt.int32
I16 = mybir.dt.int16
ALU = mybir.AluOpType
ACT = mybir.ActivationFunctionType
AX = mybir.AxisListType
WHY = "block numbers come from node numbers, which are below N_NODES"

PASSES = [
    ("gcn", D, D, True, False),
    ("gin0", D, D + 1, False, False),
    ("gin1", HID, HID, False, False),
    ("gin2", HID, HID, False, False),
    ("rel", D, D, False, False),
    ("edge", HID, HID, False, True),
]


def gnn_program(nc, x, src, dst, rel, wgt, W0, b0, inW, inb, cW1, cb1, cW2, cb2, oW, ob, rW, gamma, beta,
                eW1, eb1, eW2, eb2, ident_h, tri_h, valid_h, out):
    scratch = lambda n, s: nc.dram_tensor(n, s, F32, kind="Internal").ap()
    t_x1 = scratch("t_x1", [NB * P, D])
    t_z1 = scratch("t_z1", [NB * P, HID])
    t_z2 = scratch("t_z2", [NB * P, HID])
    t_rel = scratch("t_rel", [NB * P * RELS, D])
    t_P = scratch("t_P", [NB * P, HID])
    t_Q = scratch("t_Q", [NB * P, HID])

    with ExitStack() as ctx:
        def sb(name, shape, dt=F32):
            return ctx.enter_context(nc.sbuf_tensor(name, shape, dt))

        def sem(name):
            return ctx.enter_context(nc.semaphore(name))

        acc = sb("acc", [P, NB * HID])
        accv = acc[:, :].rearrange("p (b f) -> p b f", b=NB)
        xs = sb("xs", [P, NB, D])
        G = [sb(f"G{i}", [P, T, HID]) for i in range(2)]
        oh = [sb(f"oh{i}", [P, T, P]) for i in range(2)]
        ohx = sb("ohx", [P, T, P])
        node_id = sb("node_id", [P, NB * P], I16)
        dstT = sb("dstT", [P, T, NC])
        wT = sb("wT", [P, T, NC])
        srcI = sb("srcI", [P, T, NC], I32)
        dstI = sb("dstI", [P, T, NC], I32)
        relI = sb("relI", [P, T, NC], I32)
        col = [sb(f"col{i}", [P, T], I32) for i in range(2)]
        colp = [sb(f"colp{i}", [P, T], I32) for i in range(2)]
        meta2 = sb("meta2", [1, 3, NC + 1], I32)
        meta = sb("meta", [1, NC + 1], I32)
        ident = sb("ident", [P, P])
        ones = sb("ones", [P, P])
        tail_ones = sb("tail_ones", [P, P])
        W0s = sb("W0s", [P, 2, D])
        M0 = sb("M0", [P, 2, HID])
        M12 = sb("M12", [P, 2, 4, HID])
        N0 = sb("N0", [P, 2, D])
        N1 = sb("N1", [P, 4, D])
        N2 = sb("N2", [P, 4, D])
        N3 = sb("N3", [P, 4, D])
        Rw = sb("Rw", [P, 2, RELS * D])
        eWd, eWb, eW2s = M0, N1[:, :, :].rearrange("p a b -> p (a b)").rearrange("p (k n) -> p k n", k=2), N2
        eWa = N3[:, :, :].rearrange("p a b -> p (a b)").rearrange("p (k n) -> p k n", k=2)
        GP = [M12[:, i, :, :] for i in range(2)]
        b0b = sb("b0b", [P, D])
        cB = [sb(f"cB{i}", [P, HID]) for i in range(3)]
        b1B = [sb(f"b1B{i}", [P, HID]) for i in range(3)]
        obB = sb("obB", [P, D])
        gamB = sb("gamB", [P, D])
        betB = sb("betB", [P, D])
        eb1B = sb("eb1B", [P, HID])
        eb2B = sb("eb2B", [P, D])
        degp1 = sb("degp1", [P, NB])
        deg = sb("deg", [P, NB])
        rdeg = sb("rdeg", [P, NB])
        ub = sb("ub", [P, HID])
        uT = sb("uT", [P, 4, P])
        tt = sb("tt", [P, HID])
        t2 = sb("t2", [P, HID])
        zb = sb("zb", [P, HID])
        zT = sb("zT", [P, 4, P])
        xb = sb("xb", [P, D])
        xT = sb("xT", [P, 2, P])
        big = sb("big", [P, RELS * D])
        st = sb("st", [P, 6])
        mv = sb("mv", [P, 2])
        sd = sb("sd", [P, 1])
        rstd = sb("rstd", [P, 1])
        epsc = sb("epsc", [P, 1])

        at = [0]

        def temp(n, parts=P):
            a = acc[0:parts, at[0]:at[0] + n]
            at[0] += n
            return a
        fX = temp(2048).rearrange("p (k n) -> p k n", k=4)
        fXT = temp(2048).rearrange("p (k n) -> p k n", k=4)
        fY = temp(2048).rearrange("p (k n) -> p k n", k=4)
        fO = temp(1024).rearrange("p (k n) -> p k n", k=4)
        fbc = temp(4)
        fB = temp(512).rearrange("p (k n) -> p k n", k=4)
        raw = {n: temp(CE, NC) for n in ("dst", "src", "rel", "wgt")}
        flt = {n: (raw[n] if n == "wgt" else xs[0:NC, 2 * i:2 * i + 2, :].rearrange("p a b -> p (a b)"))
               for i, n in enumerate(("dst", "src", "rel", "wgt"))}
        valid = temp(T * NC).rearrange("p (j c) -> p j c", j=T)
        relF = temp(T * NC).rearrange("p (j c) -> p j c", j=T)
        dtmp = temp(T * NC).rearrange("p (j c) -> p j c", j=T)
        identc = temp(NC + 1, NC)
        tri = temp(NC + 1, NC)
        shift = temp(NC + 1, NC)
        lohi = temp(8, NC)
        lohi_i = lohi.bitcast(I32)
        assert at[0] <= NB * HID

        bank = [ctx.enter_context(nc.psum_tensor(f"bank{i}", [P, 512], F32)) for i in range(8)]
        ps_main, ps_extra = bank[0:2], bank[2]
        ps_uT, ps_u, ps_zT, ps_z, ps_r = bank[3], bank[4], bank[5], bank[6], bank[7]

        s_in = sem("s_in")
        s_w = sem("s_w")
        s_cast = sem("s_cast")
        s_tr = sem("s_tr")
        s_idx = sem("s_idx")
        s_meta = sem("s_meta")
        s_mps = sem("s_mps")
        s_const = sem("s_const")
        s_fx = sem("s_fx")
        s_ft = sem("s_ft")
        s_fc = sem("s_fc")
        s_fb = sem("s_fb")
        s_fm = sem("s_fm")
        s_fe = sem("s_fe")
        s_clear = sem("s_clear")
        s_e = sem("s_e")
        s_ed = sem("s_ed")
        s_held = sem("s_held")
        s_eps = sem("s_eps")
        s_bn = sem("s_bn")
        s_out = sem("s_out")

        class PassSems:
            def __init__(self, p, n):
                self.gath = [sem(f"{n}_gath{i}") for i in range(2)]
                self.colr = sem(f"{n}_col")
                self.oh = sem(f"{n}_oh")
                self.main = sem(f"{n}_main")
                self.ohx = sem(f"{n}_ohx")
                self.extra = sem(f"{n}_extra")
                self.added = sem(f"{n}_added")
                self.hid = sem(f"{n}_hid") if p in (4, 5) else None
                self.sum = sem(f"{n}_sum") if p in (5,) else None
                self.src = sem(f"{n}_src")
                self.ut = sem(f"{n}_ut")
                self.utc = sem(f"{n}_utc")
                self.u = sem(f"{n}_u")
                self.uu = sem(f"{n}_uu")
                self.z = sem(f"{n}_z") if p in (0, 1, 2, 3, 4) else None
                self.zt = sem(f"{n}_zt") if p in (0, 1, 2, 3) else None
                self.ztc = sem(f"{n}_ztc") if p in (0, 1, 2, 3) else None
                self.zz = sem(f"{n}_zz") if p in (0, 1, 2, 3, 4) else None
                self.zu = sem(f"{n}_zu") if p in (0, 1, 2, 3) else None
                self.xt = sem(f"{n}_xt") if p in (3,) else None
                self.xtc = sem(f"{n}_xtc") if p in (3,) else None
                self.r = sem(f"{n}_r") if p in (3,) else None
                self.rc = sem(f"{n}_rc") if p in (3,) else None
                self.var = sem(f"{n}_var") if p in (0, 3, 4, 5) else None
                self.sd = sem(f"{n}_sd") if p in (0, 3, 4, 5) else None
                self.x = sem(f"{n}_x") if p in (0, 3, 4, 5) else None
                self.st = sem(f"{n}_st") if p in (0, 1, 2, 3, 4) else None
                self.tab = sem(f"{n}_tab") if p in (0, 1, 2, 3, 4) else None
                self.v = sem(f"{n}_v")
        S = [PassSems(p, q[0]) for p, q in enumerate(PASSES)]
        TABLES = [(x, None), (t_x1, None), (t_z1, None), (t_z2, None), (t_rel, None), (t_Q, t_P)]

        def chunks(e, body):
            body(0, 0, True, False)
            body(1, 1, True, False)
            with e.Fori(2, NC - 2, 2) as c:
                body(c, 0, False, False)
                body(c + 1, 1, False, False)
            body(NC - 2, 0, False, False)
            body(NC - 1, 1, False, True)

        def blocks(e, body):
            body(0, True)
            with e.Fori(1, NB, 1) as b:
                body(b, False)

        def read_meta(e, c):
            m = e.value_load(meta[0:1, bass.ds(c, 1)], min_val=0, max_val=1 << 28)
            first = nc.s_assert_within(e.snap(m & 31), 0, NB - 1, skip_runtime_bounds_check_because=WHY)
            more = nc.s_assert_within(e.snap((m >> 5) & 31), 0, NB - 1, skip_runtime_bounds_check_because=WHY)
            so_far = e.snap(m >> 15)
            following = nc.s_assert_within(e.snap((m >> 10) & 31), 0, NB - 1, skip_runtime_bounds_check_because=WHY)
            return first, more, so_far, following

        def block_of(first, i):
            return nc.s_assert_within(first + i, 0, NB - 1, skip_runtime_bounds_check_because=WHY)

        block = ctx.enter_context(nc.Block())

        FOLDS = [(inW, 2, inb, 0), (cW2[0], 4, cb2[0], 1), (cW2[1], 4, cb2[1], 2), (cW2[2], 4, cb2[2], 3)]

        def fold_pieces(i):
            return sum(((k + 1) if j < 3 else 0) + k for j, (_, k, _, _) in enumerate(FOLDS[:i]))

        @block.sync
        def _(e):
            n_in = 0
            for name, a in (("dst", dst), ("src", src), ("rel", rel), ("wgt", wgt)):
                t = raw[name] if name == "wgt" else raw[name].bitcast(I32)
                full = (NC - 1) * CE
                e.dma_start(t[0:NC - 1, :], a[0:full].rearrange("(c e) -> c e", e=CE)).then_inc(s_in, 16)
                e.dma_start(t[NC - 1:NC, 0:LAST], a[full:EDGES].rearrange("(c e) -> c e", c=1)).then_inc(s_in, 16)
                e.dma_start(t[NC - 1:NC, LAST:CE], a[full:full + CE - LAST].rearrange("(c e) -> c e", c=1)).then_inc(s_in, 16)
            e.dma_start(ident[:], ident_h).then_inc(s_in, 16)
            e.dma_start(identc, tri_h[0]).then_inc(s_in, 16)
            e.dma_start(tri, tri_h[1]).then_inc(s_in, 16)
            e.dma_start(shift, tri_h[2]).then_inc(s_in, 16)
            e.dma_start(valid, valid_h).then_inc(s_in, 16)
            e.dma_start(W0s[:], W0.rearrange("(k p) n -> p k n", p=P)).then_inc(s_w, 16)
            for t, a in ((b0b, b0), (b1B[0], cb1[0]), (b1B[1], cb1[1]), (b1B[2], cb1[2]), (obB, ob),
                         (gamB, gamma), (betB, beta), (eb1B, eb1), (eb2B, eb2)):
                e.dma_start(t[:], a.partition_broadcast(P)).then_inc(s_w, 16)
            for r in range(RELS):
                e.dma_start(Rw[:, :, r * D:(r + 1) * D], rW[r].rearrange("(k p) n -> p k n", p=P)).then_inc(s_w, 16)
            for i, (X, k, b, o) in enumerate(FOLDS):
                if i:
                    e.wait_ge(s_fm, fold_pieces(i))
                e.dma_start(fX[:, 0:k, :], X.rearrange("(k p) n -> p k n", p=P)).then_inc(s_fx, 16)
                if i < 3:
                    e.dma_start(fY, cW1[i].rearrange("(k p) n -> p k n", p=P)).then_inc(s_fx, 16)
                e.dma_start(fO, oW[o * HID:(o + 1) * HID, :].rearrange("(k p) n -> p k n", p=P)).then_inc(s_fx, 16)
                with nc.allow_non_contiguous_dma(reason="a bias as a column"):
                    e.dma_start(fbc, b.rearrange("(k p) -> p k", p=P)).then_inc(s_fx, 16)
            e.wait_ge(s_idx, 1)
            e.wait_ge(s_clear, 3)
            e.dma_start(xs[:, 0:NB - 1, :], x[0:(NB - 1) * P, :].rearrange("(b p) d -> p b d", p=P)).then_inc(s_in, 16)
            e.dma_start(xs[0:TAIL, NB - 1, :], x[(NB - 1) * P:N_NODES, :]).then_inc(s_in, 16)

            def store(p, b, table, rows, n_src):
                e.wait_ge(S[p].st, b + 1)
                e.dma_start(table[bass.ds(b * P, P), :], rows).then_inc(S[p].tab, 16)

            blocks(e, lambda b, first: store(0, b, t_x1, xs[:, bass.ds(b, 1), :].rearrange("p a d -> p (a d)"), 1))
            for p, table in ((1, t_z1), (2, t_z2)):
                blocks(e, lambda b, first: store(p, b, table, accv[:, bass.ds(b, 1), :].rearrange("p a d -> p (a d)"), 1))
            relv = t_rel.rearrange("(n r) d -> n (r d)", r=RELS)
            blocks(e, lambda b, first: store(3, b, relv, big[:, :], 1))
            e.wait_ge(S[3].zu, NB)
            e.dma_start(eWa, eW1[0:D, :].rearrange("(k p) n -> p k n", p=P)).then_inc(s_e, 16)
            e.dma_start(eWb, eW1[D:2 * D, :].rearrange("(k p) n -> p k n", p=P)).then_inc(s_e, 16)
            e.dma_start(eW2s[:], eW2.rearrange("(k p) n -> p k n", p=P)).then_inc(s_e, 16)

            def store_pq(b, first):
                e.wait_ge(S[4].st, 2 * b + 2)
                e.dma_start(t_P[bass.ds(b * P, P), :], big[:, 0:HID]).then_inc(S[4].tab, 16)
                e.dma_start(t_Q[bass.ds(b * P, P), :], big[:, HID:2 * HID]).then_inc(S[4].tab, 16)
            blocks(e, store_pq)
            e.wait_ge(S[5].x, NB)
            e.dma_start(out[0:(NB - 1) * P, :].rearrange("(b p) d -> p b d", p=P), xs[:, 0:NB - 1, :]).then_inc(s_out, 16)
            e.dma_start(out[(NB - 1) * P:N_NODES, :], xs[0:TAIL, NB - 1, :]).then_inc(s_out, 16)
            e.wait_ge(s_out, 32)

        @block.gpsimd
        def _(e):
            e.iota(node_id[:, :], [[1, NB * P]], 0, 0).then_inc(s_const, 1)
            e.memset(ones[:], 1.0).then_inc(s_const, 1)
            e.memset(tail_ones[:], 0.0).then_inc(s_const, 1)
            e.wait_ge(s_const, 3)
            e.affine_select(out=tail_ones[:], in_=tail_ones[:], compare_op=ALU.is_ge, fill=1.0, base=-TAIL,
                            pattern=[[0, P]], channel_multiplier=1).then_inc(s_const, 1)
            e.wait_ge(s_idx, 5)
            for p, (name, wg, _, _, two) in enumerate(PASSES):
                if p:
                    e.wait_ge(S[p - 1].tab, 16 * NB * (2 if two else 1))
                if p == 5:
                    e.wait_ge(S[3].u, NB)
                rows = relI if name == "rel" else srcI

                def gather(c, slot, first, last_chunk):
                    s = S[p]
                    if not first:
                        e.wait_ge(s.main, c - 1)
                    e.tensor_copy(col[slot][:], rows[:, :, bass.ds(c, 1)].rearrange("p j c -> p (j c)")).then_inc(s.colr, 1)
                    if two:
                        e.tensor_copy(colp[slot][:], dstI[:, :, bass.ds(c, 1)].rearrange("p j c -> p (j c)")).then_inc(s.colr, 1)
                    e.wait_ge(s.colr, (c + 1) * (2 if two else 1))
                    e.sem_inc(s_held, 1)
                    for j in range(T):
                        e.indirect_dma_start(
                            G[slot][:, j, 0:wg], None, TABLES[p][0],
                            bass.IndirectOffsetOnAxis(ap=col[slot][:, j:j + 1], axis=0)).then_inc(s.gath[slot], 16)
                        if two:
                            e.indirect_dma_start(
                                GP[slot][:, j, :], None, TABLES[p][1],
                                bass.IndirectOffsetOnAxis(ap=colp[slot][:, j:j + 1], axis=0)).then_inc(s.gath[slot], 16)
                chunks(e, gather)

        def transposes(e, dst_bank, src_rows, k):
            for i in range(k):
                last = e.transpose(dst_bank[:, i * P:(i + 1) * P], src_rows[:, i * P:(i + 1) * P], ident[:])
            return last

        def product(e, out_ap, lhsT, rhs, k):
            for i in range(k):
                last = e.matmul(out_ap, lhsT[:, i, :], rhs(i), start=(i == 0), stop=(i == k - 1))
            return last

        @block.tensor
        def _(e):
            e.wait_ge(s_in, 16 * 17)
            e.wait_ge(s_cast, 3)
            for q, name in enumerate(("dst", "src", "rel", "wgt")):
                for j in range(T):
                    last = e.transpose(bank[q][:, j * NC:(j + 1) * NC], flt[name][:, j * P:(j + 1) * P],
                                       identc[:, 0:NC])
                last.then_inc(s_tr, 1)
            e.wait_ge(s_meta, 7)
            e.matmul(bank[7][0:1, 0:NC + 1], lohi[:, 4:5], identc, start=True, stop=False)
            e.matmul(bank[7][0:1, 0:NC + 1], lohi[:, 7:8], shift, start=False, stop=True)
            e.matmul(bank[7][0:1, 128:128 + NC + 1], lohi[:, 6:7], tri, start=True, stop=True).then_inc(s_mps, 1)
            e.wait_ge(s_meta, 9)
            e.wait_ge(s_idx, 5)
            n = nx = 0
            for i, (X, k, b, o) in enumerate(FOLDS):
                nx += 4 if i < 3 else 3
                e.wait_ge(s_fx, 16 * nx)
                for r in range(k):
                    if n + r >= 2:
                        e.wait_ge(s_fe, n + r - 1)
                    for m in range(4):
                        last = e.transpose(bank[(n + r) % 2][:, m * P:(m + 1) * P], fX[:, r, m * P:(m + 1) * P], ident[:])
                    last.then_inc(s_ft, 1)
                n += k
                e.wait_ge(s_fe, n)
                e.wait_ge(s_fb, 4 * (i + 1))
                for m in range(4):
                    e.matmul(bank[6][:, 0:D], fB[:, m, :], fO[:, m, :], start=(i == 0 and m == 0), stop=(i == 3 and m == 3))
                for Y, width in ((fY, HID), (fO, D)) if i < 3 else ((fO, D),):
                    for r in range(k):
                        e.wait_ge(s_fe, n - 1)
                        for m in range(4):
                            last = e.matmul(bank[n % 2][:, 0:width], fXT[:, m, r * P:(r + 1) * P], Y[:, m, :],
                                            start=(m == 0), stop=(m == 3))
                        last.then_inc(s_fm, 1)
                        n += 1
                    if width == HID:
                        e.wait_ge(s_fe, n - 1)
                        for m in range(4):
                            last = e.matmul(bank[n % 2][:, 0:HID], fB[:, m, :], Y[:, m, :], start=(m == 0), stop=(m == 3))
                        last.then_inc(s_fm, 1)
                        n += 1
            e.wait_ge(s_clear, 4)

            for p, (name, wg, ws, _, two) in enumerate(PASSES):
                s = S[p]

                def pair(c, slot, first, last_chunk):
                    _, more, so_far, _ = read_meta(e, c)
                    e.wait_ge(s.gath[slot], (c - slot + 2) * (8 * T * (2 if two else 1)))
                    if two:
                        e.wait_ge(s.hid, c + 1)
                    with e.If(more > 0):
                        with e.Fori(1, more + 1, 1) as i:
                            e.wait_ge(s.ohx, so_far + i)
                            for j in range(T):
                                last = e.matmul(ps_extra[:, 0:ws], ohx[:, j, :], G[slot][:, j, 0:ws], start=(j == 0), stop=(j == T - 1))
                            last.then_inc(s.extra, 1)
                    e.wait_ge(s.oh, c + 1)
                    if not first:
                        e.wait_ge(s.added, c + so_far)
                    for j in range(T):
                        last = e.matmul(ps_main[slot][:, 0:ws], oh[slot][:, j, :], G[slot][:, j, 0:ws], start=(j == 0), stop=(j == T - 1))
                    last.then_inc(s.main, 1)
                chunks(e, pair)

                k1 = 4 if ws == HID else 2
                if p in (0, 1, 2, 3, 5):
                    w1, n1 = [(W0s, D), (M0, HID), (M12[:, 0], HID), (M12[:, 1], HID), None, (eW2s, D)][p]
                    w2, k2 = [(N0, 2), (N1, 4), (N2, 4), (N3, 4), None, (None, 0)][p]

                    def finish(b, first):
                        e.wait_ge(s.src, b + 1)
                        if not first:
                            e.wait_ge(s.utc, b)
                        transposes(e, ps_uT, ub, k1).then_inc(s.ut, 1)
                        e.wait_ge(s.utc, b + 1)
                        if not first:
                            e.wait_ge(s.uu, b)
                        product(e, ps_u[:, 0:n1], uT, lambda i: w1[:, i, :], k1).then_inc(s.u, 1)
                        if w2 is not None:
                            e.wait_ge(s.z, b + 1)
                            if not first:
                                e.wait_ge(s.xtc if p == 3 else s.ztc, b)
                            transposes(e, ps_zT, zb, k2).then_inc(s.zt, 1)
                            e.wait_ge(s.ztc, b + 1)
                            if not first:
                                e.wait_ge(s.zu, b)
                            product(e, ps_z[:, 0:D], zT, lambda i: w2[:, i, :], k2).then_inc(s.zz, 1)
                        if p == 3:
                            e.wait_ge(s.x, b + 1)
                            transposes(e, ps_zT, xb, 2).then_inc(s.xt, 1)
                            e.wait_ge(s.xtc, b + 1)
                            for q in range(4):
                                if q or not first:
                                    e.wait_ge(s.rc, 4 * b + q)
                                product(e, ps_r[:, :], xT, lambda i: Rw[:, i, q * 512:(q + 1) * 512], 2).then_inc(s.r, 1)
                    blocks(e, finish)
                else:
                    e.wait_ge(s_bn, 1)
                    e.matmul(ps_z[:, 0:D], ones[:], accv[:, 0, 0:D], start=True, stop=False)
                    with e.Fori(1, NB - 1, 1) as b:
                        e.matmul(ps_z[:, 0:D], ones[:], accv[:, bass.ds(b, 1), 0:D].rearrange("p a d -> p (a d)"), start=False, stop=False)
                    e.matmul(ps_z[:, 0:D], ones[:], accv[:, NB - 1, 0:D], start=False, stop=True).then_inc(s_bn, 1)
                    e.wait_ge(s.uu, NB)
                    e.matmul(ps_r[:, 0:D], ones[:], accv[:, 0, D:2 * D], start=True, stop=False)
                    with e.Fori(1, NB - 1, 1) as b:
                        e.matmul(ps_r[:, 0:D], ones[:], accv[:, bass.ds(b, 1), D:2 * D].rearrange("p a d -> p (a d)"), start=False, stop=False)
                    e.matmul(ps_r[:, 0:D], tail_ones[:], accv[:, NB - 1, D:2 * D], start=False, stop=True).then_inc(s_bn, 1)
                    e.wait_ge(s_ed, 1)

                    def finish_bn(b, first):
                        e.wait_ge(s.x, b + 1)
                        if not first:
                            e.wait_ge(s.utc, b)
                        transposes(e, ps_uT, xb, 2).then_inc(s.ut, 1)
                        e.wait_ge(s.utc, b + 1)
                        if first:
                            e.wait_ge(s_bn, 4)
                        else:
                            e.wait_ge(s.st, 2 * b)
                        product(e, ps_u[:, :], uT, lambda i: eWd[:, i, :], 2).then_inc(s.u, 1)
                        product(e, ps_z[:, :], uT, lambda i: eWb[:, i, :], 2).then_inc(s.zz, 1)
                    blocks(e, finish_bn)

        @block.scalar
        def _(e):
            n = 0
            for i, (X, k, b, o) in enumerate(FOLDS):
                for r in range(k):
                    e.wait_ge(s_ft, sum(f[1] for f in FOLDS[:i]) + r + 1)
                    if i and r == 0:
                        e.wait_ge(s_fm, fold_pieces(i))
                    e.activation(fXT[:, :, r * P:(r + 1) * P], bank[n % 2][:, :].rearrange("p (m c) -> p m c", m=4),
                                 ACT.Copy).then_inc(s_fe, 1)
                    n += 1
                m = fold_pieces(i)
                outs = []
                if i < 3:
                    M = [M0, M12[:, 0], M12[:, 1]][i]
                    outs += [(M[:, r, :], HID) for r in range(k)] + [(cB[i][:], HID)]
                outs += [([N0, N1, N2, N3][i][:, r, :], D) for r in range(k)]
                for o_ap, width in outs:
                    m += 1
                    e.wait_ge(s_fm, m)
                    e.activation(o_ap, bank[n % 2][:, 0:width], ACT.Copy).then_inc(s_fe, 1)
                    n += 1

            e.wait_ge(s_eps, 1)
            for p, (name, wg, ws, _, two) in enumerate(PASSES):
                s = S[p]
                if p == 4:
                    e.wait_ge(s_bn, 4)
                    e.activation(t2[:, D:2 * D], t2[:, 0:D], ACT.Sqrt).then_inc(s.hid, 1)
                if two:
                    def hidden(c, slot, first, last_chunk):
                        e.wait_ge(s.sum, c + 1)
                        g = G[slot][:, :, :].rearrange("p j f -> p (j f)")
                        e.activation(g, g, ACT.Relu).then_inc(s.hid, 1)
                    chunks(e, hidden)
                k1 = 4 if ws == HID else 2

                def new_state(b):
                    e.wait_ge(s.var, b + 1)
                    e.activation(sd[:], mv[:, 1:2], ACT.Sqrt, bias=epsc[:, 0:1]).then_inc(s.sd, 1)

                def copies(b, first):
                    xsb = xs[:, bass.ds(b, 1), :].rearrange("p a d -> p (a d)")
                    accb = accv[:, bass.ds(b, 1), :].rearrange("p a d -> p (a d)")
                    if p == 4:
                        new_state(b)
                        e.wait_ge(s.x, b + 1)
                        e.activation(xsb, xb[:], ACT.Copy).then_inc(s.z, 1)
                    e.wait_ge(s.ut, b + 1)
                    if not first:
                        e.wait_ge(s.zz if p == 4 else s.u, b)
                    e.activation(uT[:, :, :].rearrange("p k c -> p (k c)")[:, 0:(2 if p == 4 else k1) * P],
                                 ps_uT[:, 0:(2 if p == 4 else k1) * P], ACT.Copy).then_inc(s.utc, 1)
                    if p == 4:
                        e.wait_ge(s.zz, b + 1)
                        if not first:
                            e.wait_ge(s.tab, 32 * b)
                        e.activation(big[:, HID:2 * HID], ps_z[:, :], ACT.Copy).then_inc(s.st, 1)
                        return
                    if p == 0 or p == 5:
                        new_state(b)
                    if p == 0:
                        e.wait_ge(s.x, b + 1)
                        e.activation(accb[:, 0:D], zb[:, 0:D], ACT.Copy).then_inc(s.st, 1)
                        k2 = 2
                    elif p in (1, 2, 3):
                        e.wait_ge(s.uu, b + 1)
                        if not first:
                            e.wait_ge(s.zt, b)
                        e.activation(zb[:], t2[:], ACT.Relu).then_inc(s.z, 1)
                        if p < 3:
                            e.activation(accb, t2[:], ACT.Relu).then_inc(s.st, 1)
                        k2 = 4
                    if p < 4:
                        e.wait_ge(s.zt, b + 1)
                        if not first:
                            e.wait_ge(s.zz, b)
                        e.activation(zT[:, :, :].rearrange("p k c -> p (k c)")[:, 0:k2 * P], ps_zT[:, 0:k2 * P],
                                     ACT.Copy).then_inc(s.ztc, 1)
                    if p == 3:
                        new_state(b)
                        e.wait_ge(s.xt, b + 1)
                        if not first:
                            e.wait_ge(s.r, 4 * b)
                        e.activation(xT[:, :, :].rearrange("p k c -> p (k c)"), ps_zT[:, 0:2 * P], ACT.Copy).then_inc(s.xtc, 1)
                        for q in range(4):
                            e.wait_ge(s.r, 4 * b + q + 1)
                            if q == 0 and not first:
                                e.wait_ge(s.tab, 16 * b)
                            a = e.activation(big[:, q * 512:(q + 1) * 512], ps_r[:, :], ACT.Copy)
                            a.then_inc(s.rc, 1)
                        e.wait_ge(s.rc, 4 * b + 4)
                        e.activation(xsb, xb[:], ACT.Copy).then_inc(s.st, 1)
                blocks(e, copies)

        @block.vector
        def _(e):
            e.memset(epsc[:], EPS).then_inc(s_eps, 1)
            e.wait_ge(s_in, 16 * 17)
            for name in ("dst", "src", "rel"):
                e.tensor_copy(flt[name], raw[name].bitcast(I32)).then_inc(s_cast, 1)
            e.wait_ge(s_cast, 3)
            e.tensor_reduce(lohi_i[:, 0:1], flt["dst"], AX.X, ALU.min).then_inc(s_meta, 1)
            e.tensor_reduce(lohi_i[:, 1:2], flt["dst"], AX.X, ALU.max).then_inc(s_meta, 1)
            e.wait_ge(s_meta, 2)
            e.tensor_scalar(lohi_i[:, 2:4], lohi_i[:, 0:2], 7, None, ALU.arith_shift_right).then_inc(s_meta, 1)
            e.wait_ge(s_meta, 3)
            e.tensor_copy(lohi[:, 0:2], lohi_i[:, 2:4]).then_inc(s_meta, 1)
            e.wait_ge(s_meta, 4)
            e.tensor_tensor(lohi[:, 6:7], lohi[:, 1:2], lohi[:, 0:1], ALU.subtract).then_inc(s_meta, 1)
            e.wait_ge(s_meta, 5)
            e.tensor_scalar(lohi[:, 7:8], lohi[:, 0:1], 1024.0, None, ALU.mult).then_inc(s_meta, 1)
            e.scalar_tensor_tensor(out=lohi[:, 4:5], in0=lohi[:, 6:7], scalar=32.0, in1=lohi[:, 0:1],
                                   op0=ALU.mult, op1=ALU.add).then_inc(s_meta, 1)
            e.wait_ge(s_tr, 4)
            pv = [bank[q][:, 0:T * NC].rearrange("p (j c) -> p j c", j=T) for q in range(4)]
            e.scalar_tensor_tensor(out=dtmp, in0=pv[0], scalar=1.0, in1=valid, op0=ALU.add, op1=ALU.mult)
            e.tensor_copy(dstI[:], pv[0])
            e.tensor_copy(srcI[:], pv[1])
            e.tensor_copy(relF, pv[2])
            e.tensor_copy(wT[:], pv[3]).then_inc(s_idx, 3)
            e.wait_ge(s_idx, 3)
            e.tensor_scalar(dstT[:], dtmp, -1.0, None, ALU.add).then_inc(s_idx, 1)
            e.scalar_tensor_tensor(out=relI[:], in0=pv[1], scalar=float(RELS), in1=relF, op0=ALU.mult, op1=ALU.add).then_inc(s_idx, 1)
            e.wait_ge(s_mps, 1)
            e.tensor_copy(meta2[:, 0, :], bank[7][0:1, 0:NC + 1]).then_inc(s_meta, 1)
            e.tensor_copy(meta2[:, 1, :], bank[7][0:1, 128:128 + NC + 1]).then_inc(s_meta, 1)
            e.wait_ge(s_meta, 9)
            e.tensor_scalar(meta2[:, 2, :], meta2[:, 1, :], 15, None, ALU.logical_shift_left).then_inc(s_meta, 1)
            e.wait_ge(s_meta, 10)
            e.tensor_tensor(meta[:], meta2[:, 0, :], meta2[:, 2, :], ALU.bitwise_or).then_inc(s_meta, 1)
            e.memset(xs[:, NB - 1, :], 0.0).then_inc(s_clear, 3)
            e.wait_ge(s_const, 4)
            nx = 0
            for i, (X, k, b, o) in enumerate(FOLDS):
                nx += 4 if i < 3 else 3
                e.wait_ge(s_fx, 16 * nx)
                for m in range(4):
                    e.tensor_scalar(fB[:, m, :], ones[:], fbc[:, m:m + 1], None, ALU.mult).then_inc(s_fb, 1)
            e.wait_ge(s_fm, fold_pieces(4))
            e.wait_ge(s_w, 16 * (10 + RELS))
            e.wait_ge(s_fe, sum(f[1] for f in FOLDS) + fold_pieces(4))
            e.tensor_tensor(obB[:], obB[:], bank[6][:, 0:D], ALU.add)
            e.memset(acc[:], 0.0)
            for i in range(2):
                e.memset(G[i][:, :, D:D + 1], 1.0)
            e.memset(st[:], 0.0).then_inc(s_clear, 1)
            e.wait_ge(s_clear, 4)
            e.memset(accv[:, :, D:D + 1], 1.0).then_inc(S[0].added, 1)

            for p, (name, wg, ws, weighted, two) in enumerate(PASSES):
                s = S[p]
                if p:
                    if p < 4:
                        e.wait_ge(S[p - 1].st, NB)
                    e.memset(st[:], 0.0).then_inc(s.added, 1)

                def one_hot(o, b, c, j_sem):
                    for j in range(T):
                        a = e.tensor_scalar(o[:, j, :], node_id[:, bass.ds(b * P, P)], dstT[:, j, bass.ds(c, 1)],
                                            wT[:, j, bass.ds(c, 1)] if weighted else None, ALU.is_equal,
                                            ALU.mult if weighted else ALU.bypass)
                    a.then_inc(j_sem, 1)

                def prepare(b, c, slot):
                    one_hot(oh[slot], b, c, s.oh)
                    if two:
                        e.wait_ge(s.gath[slot], (c - slot + 2) * (16 * T))
                        e.tensor_tensor(G[slot][:], G[slot][:], GP[slot], ALU.add).then_inc(s.sum, 1)

                def add(b, ps):
                    a = accv[:, bass.ds(b, 1), 0:ws].rearrange("p a d -> p (a d)")
                    e.tensor_tensor(a, a, ps[:, 0:ws], ALU.add).then_inc(s.added, 1)

                def sums(c, slot, first, last_chunk):
                    lo, more, so_far, following = read_meta(e, c)
                    if isinstance(c, int) and c == 0:
                        prepare(lo, c, 0)
                    if not last_chunk:
                        if not (isinstance(c, int) and c == 0):
                            e.wait_ge(s.main, c)
                        prepare(following, c + 1, 1 - slot)
                    with e.If(more > 0):
                        with e.Fori(1, more + 1, 1) as i:
                            b = block_of(lo, i)
                            one_hot(ohx, b, c, s.ohx)
                            e.wait_ge(s.extra, so_far + i)
                            e.wait_ge(s.added, c + so_far + i)
                            add(b, ps_extra)
                    e.wait_ge(s.main, c + 1)
                    e.wait_ge(s.added, c + so_far + more + 1)
                    add(lo, ps_main[slot])
                chunks(e, sums)
                total = e.snap(e.value_load(meta[0:1, NC:NC + 1], min_val=0, max_val=1 << 28) >> 15)
                e.wait_ge(s.added, total + (NC + 1))

                def stepper(per, b):
                    k = [0]

                    def link(ins):
                        k[0] += 1
                        assert k[0] <= per
                        ins.then_inc(s.v, 1)
                        e.wait_ge(s.v, b * per + k[0])
                    link.count = k
                    return link

                def norm(link, v, b):
                    link(e.bn_stats(st[:], v))
                    e.sem_inc(s_held, 1)
                    e.bn_aggr(mv[:], st[:]).then_inc(s.var, 1)
                    e.wait_ge(s.sd, b + 1)
                    link(e.reciprocal(rstd[:], sd[:]))

                if p == 5:
                    e.tensor_scalar(deg[:], degp1[:], -1.0, None, ALU.add).then_inc(s_bn, 1)
                    e.wait_ge(s_bn, 5)
                    e.tensor_scalar(ub[:, 0:NB], deg[:], 1e-8, None, ALU.add).then_inc(s_bn, 1)
                    e.wait_ge(s_bn, 6)
                    e.reciprocal(rdeg[:], ub[:, 0:NB]).then_inc(s_bn, 1)
                    e.wait_ge(s_bn, 7)

                def state(b, first):
                    xsb = xs[:, bass.ds(b, 1), :].rearrange("p a d -> p (a d)")
                    accb = accv[:, bass.ds(b, 1), :].rearrange("p a d -> p (a d)")
                    PER = {0: 6, 1: 3, 2: 2, 3: 7, 5: 6}[p]
                    link = stepper(PER, b)
                    if not first:
                        e.wait_ge(s.ut, b)
                    nf = ws - ws % 2
                    e.tensor_scalar(ub[:, 0:nf], accb[:, 0:nf], 1.0, None, ALU.mult).then_inc(s.src, 1)
                    if p == 1:
                        link(e.tensor_scalar(degp1[:, bass.ds(b, 1)], accb[:, D:D + 1], 1.0, None, ALU.mult))
                    if p == 3:
                        e.wait_ge(s.src, b + 1)
                        link(e.tensor_scalar(accb, ones[:, 0:1].to_broadcast([P, HID]), 0.0, None, ALU.mult))
                    e.wait_ge(s.u, b + 1)
                    if p == 0:
                        if first:
                            e.wait_ge(s_in, 16 * 19)
                        link(e.tensor_tensor(tt[:, 0:D], ps_u[:, 0:D], xsb, ALU.add))
                        e.tensor_tensor(t2[:, 0:D], tt[:, 0:D], b0b[:], ALU.add).then_inc(s.uu, 1)
                        e.wait_ge(s.uu, b + 1)
                        norm(link, t2[:, 0:D], b)
                        if not first:
                            e.wait_ge(s.zt, b)
                            e.wait_ge(s.st, b)
                        e.tensor_scalar(zb[:, 0:D], t2[:, 0:D], mv[:, 0:1], rstd[:, 0:1], ALU.subtract, ALU.mult).then_inc(s.z, 1)
                        e.wait_ge(s.z, b + 1)
                        e.tensor_scalar(xsb, zb[:, 0:D], 1.0, None, ALU.mult).then_inc(s.x, 1)
                    elif p in (1, 2, 3):
                        if not first:
                            e.wait_ge(s.st if p < 3 else s.z, b)
                        link(e.scalar_tensor_tensor(out=tt[:], in0=cB[p - 1][:], scalar=degp1[:, bass.ds(b, 1)],
                                                    in1=ps_u[:, :], op0=ALU.mult, op1=ALU.add))
                        e.tensor_tensor(t2[:], tt[:], b1B[p - 1][:], ALU.add).then_inc(s.uu, 1)
                    else:
                        link(e.scalar_tensor_tensor(out=tt[:, 0:D], in0=eb2B[:], scalar=deg[:, bass.ds(b, 1)],
                                                    in1=ps_u[:, 0:D], op0=ALU.mult, op1=ALU.add))
                        e.scalar_tensor_tensor(out=t2[:, 0:D], in0=tt[:, 0:D], scalar=rdeg[:, bass.ds(b, 1)],
                                               in1=xsb, op0=ALU.mult, op1=ALU.add).then_inc(s.uu, 1)
                        e.wait_ge(s.uu, b + 1)
                        norm(link, t2[:, 0:D], b)
                        e.tensor_scalar(xsb, t2[:, 0:D], mv[:, 0:1], rstd[:, 0:1], ALU.subtract, ALU.mult).then_inc(s.x, 1)
                    if p < 3:
                        e.wait_ge(s.zz, b + 1)
                        if p == 0:
                            e.wait_ge(s.tab, (b + 1) * 16)
                        e.tensor_tensor(xsb, xsb, ps_z[:, 0:D], ALU.add).then_inc(s.zu, 1)
                    if p == 3:
                        e.wait_ge(s.zz, b + 1)
                        link(e.tensor_tensor(tt[:, 0:D], xsb, ps_z[:, 0:D], ALU.add))
                        e.tensor_tensor(tt[:, D:2 * D], tt[:, 0:D], obB[:], ALU.add).then_inc(s.zu, 1)
                        e.wait_ge(s.zu, b + 1)
                        norm(link, tt[:, D:2 * D], b)
                        if not first:
                            e.wait_ge(s.st, b)
                        e.tensor_scalar(xb[:], tt[:, D:2 * D], mv[:, 0:1], rstd[:, 0:1], ALU.subtract, ALU.mult).then_inc(s.x, 1)
                    while link.count[0] < PER:
                        link(e.memset(st[:], 0.0))

                if p != 4:
                    blocks(e, state)
                    continue

                e.memset(st[:], 0.0).then_inc(s_bn, 1)
                e.wait_ge(s_bn, 2)
                mean, scale = tt[:, 0:D], tt[:, D:2 * D]
                e.tensor_scalar(mean, ps_z[:, 0:D], 1.0 / N_NODES, None, ALU.mult).then_inc(s.src, 1)
                e.wait_ge(s.src, 1)

                def centre(b, first):
                    a = accv[:, bass.ds(b, 1), :].rearrange("p a d -> p (a d)")
                    e.tensor_tensor(a[:, 0:D], a[:, 0:D], mean, ALU.subtract).then_inc(s.v, 1)
                    e.wait_ge(s.v, b + 1)
                    e.tensor_tensor(a[:, D:2 * D], a[:, 0:D], a[:, 0:D], ALU.mult).then_inc(s.uu, 1)
                blocks(e, centre)
                e.wait_ge(s_bn, 3)
                e.wait_ge(S[3].st, NB)
                e.tensor_scalar(t2[:, 0:D], ps_r[:, 0:D], 1.0 / N_NODES, EPS, ALU.mult, ALU.add).then_inc(s_bn, 1)
                e.wait_ge(s_bn, 4)
                e.wait_ge(s_e, 48)
                e.tensor_tensor(eWd[:], eWa, eWb, ALU.subtract).then_inc(s_ed, 1)
                e.wait_ge(s.hid, 1)
                e.reciprocal(ub[:, 0:D], t2[:, D:2 * D]).then_inc(s.src, 1)
                e.wait_ge(s.src, 2)
                e.tensor_tensor(scale, ub[:, 0:D], gamB[:], ALU.mult).then_inc(s.src, 1)
                e.wait_ge(s.src, 3)

                def state_bn(b, first):
                    xsb = xs[:, bass.ds(b, 1), :].rearrange("p a d -> p (a d)")
                    accb = accv[:, bass.ds(b, 1), :].rearrange("p a d -> p (a d)")
                    k = [0]

                    def link(ins):
                        k[0] += 1
                        ins.then_inc(s.v, 1)
                        e.wait_ge(s.v, NB + b * 6 + k[0])
                    link(e.tensor_tensor(zb[:, 0:D], accb[:, 0:D], scale, ALU.mult))
                    link(e.tensor_tensor(zb[:, D:2 * D], zb[:, 0:D], betB[:], ALU.add))
                    link(e.tensor_tensor(t2[:, 0:D], zb[:, D:2 * D], xsb, ALU.add))
                    norm(link, t2[:, 0:D], b)
                    if not first:
                        e.wait_ge(s.ut, b)
                        e.wait_ge(s.z, b)
                    e.tensor_scalar(xb[:], t2[:, 0:D], mv[:, 0:1], rstd[:, 0:1], ALU.subtract, ALU.mult).then_inc(s.x, 1)
                    link(e.tensor_scalar(accb, ones[:, 0:1].to_broadcast([P, HID]), 0.0, None, ALU.mult))
                    e.wait_ge(s.u, b + 1)
                    if not first:
                        e.wait_ge(s.tab, 32 * b)
                    e.tensor_tensor(big[:, 0:HID], ps_u[:, :], eb1B[:], ALU.add).then_inc(s.st, 1)
                blocks(e, state_bn)


_INS = ["x", "src", "dst", "edge_type_8", "edge_weight", "L0_gnn_weight", "L0_gnn_bias", "L1_gnn_in_W", "L1_gnn_in_b",
        "L1_gnn_conv_W1", "L1_gnn_conv_b1", "L1_gnn_conv_W2", "L1_gnn_conv_b2", "L1_gnn_out_W", "L1_gnn_out_b",
        "L2_gnn_weight", "L2_gnn_gamma", "L2_gnn_beta", "L3_gnn_W1", "L3_gnn_b1", "L3_gnn_W2", "L3_gnn_b2"]


def shape_constants():
    import numpy as np
    ident = np.eye(P, dtype=np.float32)
    tri = np.zeros((3, NC, NC + 1), np.float32)
    tri[2] = (np.arange(NC)[:, None] == np.arange(NC + 1)[None] + 1).astype(np.float32)
    tri[0, :, :NC] = np.eye(NC)
    tri[1] = (np.arange(NC)[:, None] < np.arange(NC + 1)[None]).astype(np.float32)
    edge = np.arange(NC)[None, None] * CE + np.arange(T)[None, :, None] * P + np.arange(P)[:, None, None]
    return {"ident": ident, "tri": tri, "valid": (edge < EDGES).astype(np.float32)}


def kernel(**inputs):
    import numpy as np
    import concourse.bacc as bacc
    from concourse.bass_utils import run_bass_kernel_spmd

    nc = bacc.Bacc("TRN2", target_bir_lowering=False, num_devices=1)
    arrays, args = {}, []
    for name, a in [(n, np.ascontiguousarray(inputs[n])) for n in _INS] + list(shape_constants().items()):
        arrays[f"in_{name}"] = a
        args.append(nc.dram_tensor(f"in_{name}", a.shape, mybir.dt.from_np(a.dtype), kind="ExternalInput").ap())
    out = nc.dram_tensor("out_0", (N_NODES, D), F32, kind="ExternalOutput").ap()
    gnn_program(nc, *args, out)
    r = run_bass_kernel_spmd(nc, [arrays], core_ids=[0])
    return r.results[0]["out_0"]
```
